# Optimizing a Trainium2 kernel written in Bass

```python
import numpy as np
import jax
import jax.numpy as jnp

def _softmax(x, axis=-1):
    return jax.nn.softmax(x, axis=axis)
def _gelu(x):
    return jax.nn.gelu(x, approximate=True)
def _silu(x):
    return jax.nn.silu(x)
def _sigmoid(x):
    return jax.nn.sigmoid(x)
def _layernorm(x, axis=-1, eps=1e-5):
    m = jnp.mean(x, axis=axis, keepdims=True)
    v = jnp.var(x, axis=axis, keepdims=True)
    return (x - m) / jnp.sqrt(v + eps)
def _scatter_add(tgt, idx, src, axis=0):
    return tgt.at[idx].add(src)
def _segment_sum(src, seg, n):
    return jax.ops.segment_sum(src, seg, n)

kernel_name = 'mk_conv_preact_d1_conv_nchw32_8ea0cf'

def setup_inputs(seed: int = 0):
    np.random.seed(seed)
    _w = jnp.asarray
    def _rec_inputs():
        import jax
        import jax.numpy as jnp
        _gk = jax.random.key(seed)
        x = 0.007807 + 0.1251 * jax.random.normal(jax.random.fold_in(_gk, 1), (32, 32, 128, 128), jnp.float32)
        return x
    x = _rec_inputs()
    def _L0_conv_setup():
        import jax, jax.numpy as jnp
        import numpy as np
        NUM_ITER = 5
        B_S, C, N_C = (32, 32, 128)
        key = jax.random.key(seed)
        X = jax.random.normal(key, (B_S, C, N_C, N_C), dtype=jnp.float32)
        A = jnp.einsum('bcij,bckj->bcik', X, X) / N_C
        A = A + 0.001 * jnp.eye(N_C, dtype=jnp.float32)
        return {'A': A}
    _L0_conv_all = _L0_conv_setup()
    _L0_conv_in = {k: v for k, v in _L0_conv_all.items() if k in ()}
    del _L0_conv_all

    return {
        "x": x,
    }

def reference(x):
    import jax
    import jax.numpy as jnp
    def _L0_conv_ref(A):
        import jax, jax.numpy as jnp
        import numpy as np
        NUM_ITER = 5
        B_S, C, N_C = (32, 32, 128)
        b_s, c, n_c, _ = A.shape
        A2 = A.reshape(b_s * c, n_c, n_c)
        normA = jnp.sqrt(jnp.sum(A2 * A2, axis=(1, 2)))
        Y = A2 / normA[:, None, None]
        I = jnp.eye(n_c, dtype=A.dtype)[None]
        Z = jnp.broadcast_to(I, A2.shape)
        for _ in range(NUM_ITER):
            T = 0.5 * (3.0 * I - jnp.matmul(Z, Y))
            Y = jnp.matmul(Y, T)
            Z = jnp.matmul(T, Z)
        sA = Y * jnp.sqrt(normA)[:, None, None]
        return sA.reshape(b_s, c, n_c, n_c)

    def _gn(v, G=16, eps=1e-5):
        B_, C_, H_, W_ = v.shape
        g = v.reshape(B_, G, C_ // G, H_, W_)
        m = jnp.mean(g, axis=(2, 3, 4), keepdims=True)
        s = jnp.var(g, axis=(2, 3, 4), keepdims=True)
        return ((g - m) / jnp.sqrt(s + eps)).reshape(v.shape)

    def _ln_c(v, eps=1e-6):
        m = jnp.mean(v, axis=1, keepdims=True)
        s = jnp.var(v, axis=1, keepdims=True)
        return (v - m) / jnp.sqrt(s + eps)

    def _ln_t(v, eps=1e-5):
        m = jnp.mean(v, axis=-1, keepdims=True)
        s = jnp.var(v, axis=-1, keepdims=True)
        return (v - m) / jnp.sqrt(s + eps)

    def _to_tokens(v):
        B_, C_, H_, W_ = v.shape
        return v.reshape(B_, C_, H_ * W_).transpose(0, 2, 1)
    def _from_tokens(t, like):
        B_, C_, H_, W_ = like.shape
        return t.transpose(0, 2, 1).reshape(B_, C_, H_, W_)

    x = x + _L0_conv_ref(_gn(x))
    return x


_drawn_inputs = setup_inputs


def setup_inputs(seed=0):
    import zlib

    import numpy as np

    out = dict(_drawn_inputs(seed))
    spreads = {}
    factors = {}
    for name, (base, spread) in spreads.items():
        noise = np.random.default_rng([zlib.crc32(name.encode()), seed]).standard_normal(out[name].shape)
        drawn = base * np.exp(spread * noise) if base else spread * noise
        out[name] = jnp.asarray(drawn.astype(out[name].dtype))
    for name, factor in factors.items():
        out[name] = (out[name] * factor).astype(out[name].dtype)
    return out
```

```python
from contextlib import ExitStack

import concourse.bass as bass
from concourse import mybir

F32 = mybir.dt.float32
ALU = mybir.AluOpType
ACT = mybir.ActivationFunctionType
AX_X = mybir.AxisListType.X

N = 128
BATCH_MATS = 4
BATCHES = 4
STEP_MATS = BATCH_MATS * BATCHES
GROUP_MATS = 2
GROUPS = STEP_MATS // GROUP_MATS
GN_EPS = 1e-5
BN = 6

P1, P0 = -4.5, 3.375
H1, H0 = -8.625, 24.609375
Q_SCALE = 16.0


def newton_schulz_kernel(nc, x, out):
    mats = x.shape[0] * x.shape[1]
    steps = mats // STEP_MATS
    pairs = steps // 2
    assert steps % 2 == 0 and pairs >= 3 and x.shape[2] == x.shape[3] == N

    x_dram = x.rearrange("b c i j -> (b c) i j").rearrange("(k h m) i j -> k h i m j", h=2, m=STEP_MATS)
    out_dram = out.rearrange("b c i j -> (b c) i j").rearrange("(k h m) i j -> k h i m j", h=2, m=STEP_MATS)

    with ExitStack() as ctx:
        def sb(name, shape, dt=F32):
            return ctx.enter_context(nc.sbuf_tensor(name, shape, dt))

        def sem(name):
            return ctx.enter_context(nc.semaphore(name))

        x_sb = sb("x_sb", [N, 2, STEP_MATS, N])
        out_sb = sb("out_sb", [N, 2, STEP_MATS, N])
        a_n = sb("a_n", [N, STEP_MATS, N])
        a_t = sb("a_t", [N, STEP_MATS, N])
        g1 = sb("g1", [N, STEP_MATS, N])
        h1 = sb("h1", [N, STEP_MATS, N])
        p_n = sb("p_n", [N, STEP_MATS, N])
        p_t = sb("p_t", [N, STEP_MATS, N])
        z_n = sb("z_n", [N, STEP_MATS, N])
        wy_t = sb("wy_t", [N, STEP_MATS, 2, N])
        w_n = sb("w_n", [N, STEP_MATS, N])
        g2 = sb("g2", [N, STEP_MATS, N])
        h2 = sb("h2", [N, STEP_MATS, N])
        q_n = sb("q_n", [N, STEP_MATS, N])
        vy_t = sb("vy_t", [N, STEP_MATS, 2, N])
        t5_n = sb("t5_n", [N, STEP_MATS, N])
        eye = sb("eye", [N, BATCH_MATS, N])
        eye_p0 = sb("eye_p0", [N, BATCH_MATS, N])
        eye_h0 = sb("eye_h0", [N, BATCH_MATS, N])
        eye_15 = sb("eye_15", [N, BATCH_MATS, N])
        mean_w = sb("mean_w", [N, N])
        sum_w = sb("sum_w", [N, N])

        stats = sb("stats", [N, STEP_MATS, BN])
        mean_sum = sb("mean_sum", [N, GROUPS])
        mean = sb("mean", [N, GROUPS])
        dev = sb("dev", [N, GROUPS, 4])
        dev_sq = sb("dev_sq", [N, GROUPS, 4])
        sq_part = sb("sq_part", [N, GROUPS, 4])
        sq_row = sb("sq_row", [N, STEP_MATS])
        var_eps = sb("var_eps", [N, GROUPS])
        group_sq = sb("group_sq", [N, GROUPS])
        roots_sq = sb("roots_sq", [N, STEP_MATS + GROUPS])
        roots_0 = sb("roots_0", [N, STEP_MATS + GROUPS])
        roots_inv = sb("roots_inv", [N, STEP_MATS + GROUPS])
        roots_quot = sb("roots_quot", [N, STEP_MATS + GROUPS])
        roots_2x = sb("roots_2x", [N, STEP_MATS + GROUPS])
        half_inv = sb("half_inv", [N, STEP_MATS])
        a_scale = sb("a_scale", [N, STEP_MATS])
        fourth_0 = sb("fourth_0", [N, STEP_MATS])
        fourth_inv = sb("fourth_inv", [N, STEP_MATS])
        fourth_quot = sb("fourth_quot", [N, STEP_MATS])
        fourth_sum = sb("fourth_sum", [N, STEP_MATS])
        out_scale = sb("out_scale", [N, 2, STEP_MATS])

        bank = [ctx.enter_context(nc.psum_tensor(f"bank{i}", [N, BATCH_MATS, N], F32)) for i in range(8)]
        extra = [bank[BATCHES + b % 2] for b in range(BATCHES)]
        mean_ps = bank[6][:, 0, 0:GROUPS]
        sq_ps = bank[7][:, 0, 0:STEP_MATS]

        x_loaded = [sem("x_loaded_even"), sem("x_loaded_odd")]
        out_stored = [sem("out_stored_even"), sem("out_stored_odd")]
        consts_ready, eye_zeroed, eye_ready = sem("consts_ready"), sem("eye_zeroed"), sem("eye_ready")
        at_ps, at_ready = sem("at_ps"), sem("at_ready")
        aa_ps, p1_ready = sem("aa_ps"), sem("p1_ready")
        pt1_ps, pt1_ready = sem("pt1_ps"), sem("pt1_ready")
        pp1_ps, z_ready = sem("pp1_ps"), sem("z_ready")
        y2t_ps, y2t_ready = sem("y2t_ps"), sem("y2t_ready")
        w2_ps, w_ready = sem("w2_ps"), sem("w_ready")
        wt_ps, wt_ready = sem("wt_ps"), sem("wt_ready")
        ww_ps, p2_ready = sem("ww_ps"), sem("p2_ready")
        pt2_ps, pt2_ready = sem("pt2_ps"), sem("pt2_ready")
        pp2_ps, q_ready = sem("pp2_ps"), sem("q_ready")
        vy_ps, vy_ready = sem("vy_ps"), sem("vy_ready")
        w4_ps, t5_ready = sem("w4_ps"), sem("t5_ready")
        y5_ps, out_ready = sem("y5_ps"), sem("out_ready")
        g1_scaled, h1_scaled, g1_ready, h1_ready = sem("g1_scaled"), sem("h1_scaled"), sem("g1_ready"), sem("h1_ready")
        gh2_ready = sem("gh2_ready")
        a_ready = sem("a_ready")
        stats_done, mean_summed, mean_ps_ready, mean_ready = (
            sem("stats_done"), sem("mean_summed"), sem("mean_ps_ready"), sem("mean_ready"))
        small = sem("small")
        sq_summed, sq_ps_ready = sem("sq_summed"), sem("sq_ps_ready")
        roots_in, roots_out = sem("roots_in"), sem("roots_out")
        norm_ready, fourth_out = sem("norm_ready"), sem("fourth_out")

        def mm(b):
            return range(b * BATCH_MATS, (b + 1) * BATCH_MATS)

        def bs(b):
            return slice(b * BATCH_MATS, (b + 1) * BATCH_MATS)

        def batches_done(k, h, b):
            return k * (2 * BATCHES) + (h * BATCHES + b + 1)

        def steps_done(k, h):
            return k * 2 + (h + 1)

        def before(k, h):
            if h == 1:
                return k, 0
            return None if isinstance(k, int) and k == 0 else (k - 1, 1)

        def after(k, h):
            if h == 0:
                return k, 1
            return None if isinstance(k, int) and k == pairs - 1 else (k + 1, 0)

        def all_steps(eng, step):
            for h in range(2):
                step(0, h)
            with eng.Fori(1, pairs - 1) as k:
                for h in range(2):
                    step(k, h)
            for h in range(2):
                step(pairs - 1, h)

        block = ctx.enter_context(nc.Block())

        @block.sync
        def _(sp):
            def load(k, h):
                for b in range(BATCHES):
                    sp.dma_start(x_sb[:, h, bs(b)], x_dram[k, h, :, bs(b)]).then_inc(x_loaded[h], 16)

            for h in range(2):
                load(0, h)

            def step(k, h):
                for b in range(BATCHES):
                    sp.wait_ge(out_ready, batches_done(k, h, b))
                    sp.dma_start(out_dram[k, h, :, bs(b)], out_sb[:, h, bs(b)]).then_inc(out_stored[h], 16)
                if not (isinstance(k, int) and k == pairs - 1):
                    load(k + 1, h)

            all_steps(sp, step)
            for h in range(2):
                sp.wait_ge(out_stored[h], 16 * BATCHES * pairs)

        @block.gpsimd
        def _(pool):
            nc.gpsimd.memset(eye[:], 0.0).then_inc(eye_zeroed, 1)
            pool.wait_ge(eye_zeroed, 1)
            nc.gpsimd.affine_select(out=eye[:], in_=eye[:], compare_op=ALU.not_equal, fill=1.0, base=0,
                                    pattern=[[0, BATCH_MATS], [-1, N]], channel_multiplier=1).then_inc(eye_ready, 1)
            pool.wait_ge(consts_ready, 5)

            def poly_terms(k, h):
                for b in range(BATCHES):
                    done = batches_done(k, h, b)
                    pool.wait_ge(g1_scaled, done)
                    nc.gpsimd.tensor_tensor(g1[:, bs(b)], g1[:, bs(b)], eye_p0[:], ALU.add).then_inc(g1_ready, 1)
                    pool.wait_ge(h1_scaled, done)
                    nc.gpsimd.tensor_tensor(h1[:, bs(b)], h1[:, bs(b)], eye_h0[:], ALU.add).then_inc(h1_ready, 1)

            poly_terms(0, 0)

            def step(k, h):
                if after(k, h):
                    poly_terms(*after(k, h))

            all_steps(pool, step)

        @block.scalar
        def _(act):
            def roots(k, h):
                done = steps_done(k, h)
                act.wait_ge(roots_in, done)
                nc.scalar.activation(roots_0[:], roots_sq[:], ACT.Sqrt).then_inc(roots_out, 1)

            def fourth_roots(k, h):
                act.wait_ge(norm_ready, steps_done(k, h))
                nc.scalar.activation(fourth_0[:], roots_2x[:, 0:STEP_MATS], ACT.Sqrt, scale=0.5).then_inc(fourth_out, 1)

            def copies(k, h, src_ps, dst, ready, scale=1.0):
                for b in range(BATCHES):
                    act.wait_ge(src_ps, batches_done(k, h, b))
                    nc.scalar.activation(dst(b), bank[b][:], ACT.Copy, scale=scale).then_inc(ready, 1)

            def poly_multiples(k, h):
                prev = before(k, h)
                for b in range(BATCHES):
                    act.wait_ge(a_ready, batches_done(k, h, b))
                    if prev:
                        act.wait_ge(p1_ready, batches_done(*prev, b))
                    nc.scalar.activation(g1[:, bs(b)], a_n[:, bs(b)], ACT.Copy, scale=P1).then_inc(g1_scaled, 1)
                    if prev:
                        act.wait_ge(z_ready, batches_done(*prev, b))
                    nc.scalar.activation(h1[:, bs(b)], a_n[:, bs(b)], ACT.Copy, scale=H1).then_inc(h1_scaled, 1)

            def step(k, h):
                copies(k, h, at_ps, lambda b: a_t[:, bs(b)], at_ready)
                copies(k, h, pt1_ps, lambda b: p_t[:, bs(b)], pt1_ready)
                copies(k, h, y2t_ps, lambda b: wy_t[:, bs(b), 1], y2t_ready)
                copies(k, h, w2_ps, lambda b: w_n[:, bs(b)], w_ready, 1.0 / Q_SCALE ** 2)
                copies(k, h, wt_ps, lambda b: wy_t[:, bs(b), 0], wt_ready)
                copies(k, h, pt2_ps, lambda b: p_t[:, bs(b)], pt2_ready)
                if after(k, h):
                    roots(*after(k, h))
                    fourth_roots(*after(k, h))
                for b in range(BATCHES):
                    act.wait_ge(vy_ps, batches_done(k, h, b))
                    for i, ps in enumerate((bank[b], extra[b])):
                        m0 = b * BATCH_MATS + 2 * i
                        nc.scalar.activation(vy_t[:, m0:m0 + 2].rearrange("p m c j -> p (m c) j"), ps[:],
                                             ACT.Copy).then_inc(vy_ready, 1)
                if after(k, h):
                    poly_multiples(*after(k, h))

            roots(0, 0)
            fourth_roots(0, 0)
            poly_multiples(0, 0)
            all_steps(act, step)

        @block.vector
        def _(dve):
            nc.vector.memset(mean_w[:], 1.0 / (4 * N)).then_inc(consts_ready, 1)
            nc.vector.memset(sum_w[:], 1.0).then_inc(consts_ready, 1)
            dve.wait_ge(eye_ready, 1)
            for tile, value in ((eye_p0, P0), (eye_h0, H0), (eye_15, 1.5)):
                nc.vector.tensor_scalar(tile[:], eye[:], value, None, ALU.mult).then_inc(consts_ready, 1)
            dve.wait_ge(consts_ready, 5)

            SMALLS = 14

            def statistics(k, h):
                dve.wait_ge(x_loaded[h], k * (16 * BATCHES) + 16 * BATCHES)
                for m in range(STEP_MATS):
                    nc.vector.bn_stats(stats[:, m], x_sb[:, h, m]).then_inc(stats_done, 1)
                dve.wait_ge(stats_done, k * (2 * STEP_MATS) + (h + 1) * STEP_MATS)
                parts = stats[:].rearrange("p (g c) (r s) -> p g (c r) s", c=GROUP_MATS, s=3)
                nc.vector.tensor_reduce(mean_sum[:], parts[:, :, :, 1], AX_X, ALU.add).then_inc(mean_summed, 1)

            def squares(k, h):
                base = k * (2 * SMALLS) + h * SMALLS
                parts = stats[:].rearrange("p (g c) (r s) -> p g (c r) s", c=GROUP_MATS, s=3)
                dve.wait_ge(mean_ps_ready, steps_done(k, h))
                nc.vector.tensor_copy(mean[:], mean_ps).then_inc(mean_ready, 1)
                dve.wait_ge(mean_ready, steps_done(k, h))
                nc.vector.tensor_tensor(dev[:], parts[:, :, :, 1],
                                        mean[:].unsqueeze(2).broadcast_to([N, GROUPS, 4]), ALU.subtract).then_inc(small, 1)
                dve.wait_ge(small, base + 1)
                nc.vector.scalar_tensor_tensor(dev_sq[:], dev[:], float(N // 2), dev[:], ALU.mult, ALU.mult).then_inc(small, 1)
                dve.wait_ge(small, base + 2)
                nc.vector.tensor_tensor(sq_part[:], parts[:, :, :, 2], dev_sq[:], ALU.add).then_inc(small, 1)
                dve.wait_ge(small, base + 3)
                nc.vector.tensor_reduce(sq_row[:], sq_part[:].rearrange("p g (c r) -> p (g c) r", r=2),
                                        AX_X, ALU.add).then_inc(sq_summed, 1)

            def scales(k, h):
                base = k * (2 * SMALLS) + h * SMALLS
                norms, rstd = slice(0, STEP_MATS), slice(STEP_MATS, STEP_MATS + GROUPS)
                by_group = sq_ps.rearrange("p (g c) -> p g c", c=GROUP_MATS)

                def of_mats(tile_ap):
                    return tile_ap.rearrange("p (g c) -> p g c", c=GROUP_MATS)

                def spread(tile_ap):
                    return tile_ap.unsqueeze(2).broadcast_to([N, GROUPS, GROUP_MATS])

                dve.wait_ge(sq_ps_ready, steps_done(k, h))
                nc.vector.tensor_reduce(group_sq[:], by_group, AX_X, ALU.add).then_inc(small, 1)
                dve.wait_ge(small, base + 4)
                nc.vector.tensor_scalar(var_eps[:], group_sq[:], 1.0 / (GROUP_MATS * N * N), GN_EPS,
                                        ALU.mult, ALU.add).then_inc(small, 1)
                dve.wait_ge(small, base + 5)
                nc.vector.reciprocal(roots_sq[:, rstd], var_eps[:]).then_inc(small, 1)
                dve.wait_ge(small, base + 6)
                nc.vector.tensor_tensor(of_mats(roots_sq[:, norms]), by_group, spread(roots_sq[:, rstd]),
                                        ALU.mult).then_inc(roots_in, 1)
                dve.wait_ge(roots_out, steps_done(k, h))
                nc.vector.reciprocal(roots_inv[:], roots_0[:]).then_inc(small, 1)
                dve.wait_ge(small, base + 7)
                nc.vector.tensor_tensor(roots_quot[:], roots_sq[:], roots_inv[:], ALU.mult).then_inc(small, 1)
                dve.wait_ge(small, base + 8)
                nc.vector.tensor_tensor(roots_2x[:], roots_quot[:], roots_0[:], ALU.add).then_inc(norm_ready, 1)
                dve.wait_ge(norm_ready, steps_done(k, h))
                nc.vector.reciprocal(half_inv[:], roots_2x[:, norms]).then_inc(small, 1)
                dve.wait_ge(small, base + 9)
                nc.vector.tensor_tensor(of_mats(a_scale[:]), of_mats(half_inv[:]), spread(roots_2x[:, rstd]),
                                        ALU.mult).then_inc(small, 1)
                dve.wait_ge(fourth_out, steps_done(k, h))
                nc.vector.reciprocal(fourth_inv[:], fourth_0[:]).then_inc(small, 1)
                dve.wait_ge(small, base + 11)
                nc.vector.scalar_tensor_tensor(fourth_quot[:], roots_2x[:, norms], 0.5, fourth_inv[:],
                                               ALU.mult, ALU.mult).then_inc(small, 1)
                dve.wait_ge(small, base + 12)
                nc.vector.tensor_tensor(fourth_sum[:], fourth_quot[:], fourth_0[:], ALU.add).then_inc(small, 1)
                dve.wait_ge(small, base + 13)
                nc.vector.tensor_scalar(out_scale[:, h], fourth_sum[:], 0.5 / Q_SCALE ** 2, None, ALU.mult).then_inc(small, 1)

            def make_a(k, h):
                dve.wait_ge(small, k * (2 * SMALLS) + (h + 1) * SMALLS)
                for m in range(STEP_MATS):
                    g = m // GROUP_MATS
                    ins = nc.vector.tensor_scalar(a_n[:, m], x_sb[:, h, m], mean[:, g:g + 1], a_scale[:, m:m + 1],
                                                  ALU.subtract, ALU.mult)
                    if m % BATCH_MATS == BATCH_MATS - 1:
                        ins.then_inc(a_ready, 1)

            def step(k, h):
                for b in range(BATCHES):
                    dve.wait_ge(g1_ready, batches_done(k, h, b))
                    dve.wait_ge(aa_ps, batches_done(k, h, b))
                    nc.vector.tensor_tensor(p_n[:, bs(b)], bank[b][:], g1[:, bs(b)], ALU.add).then_inc(p1_ready, 1)
                for b in range(BATCHES):
                    dve.wait_ge(h1_ready, batches_done(k, h, b))
                    dve.wait_ge(pp1_ps, batches_done(k, h, b))
                    nc.vector.tensor_tensor(z_n[:, bs(b)], bank[b][:], h1[:, bs(b)], ALU.add).then_inc(z_ready, 1)
                if after(k, h):
                    statistics(*after(k, h))
                for b in range(BATCHES):
                    dve.wait_ge(w_ready, batches_done(k, h, b))
                    nc.vector.scalar_tensor_tensor(g2[:, bs(b)], w_n[:, bs(b)], P1, eye_p0[:], ALU.mult, ALU.add).then_inc(gh2_ready, 1)
                    nc.vector.scalar_tensor_tensor(h2[:, bs(b)], w_n[:, bs(b)], H1, eye_h0[:], ALU.mult, ALU.add).then_inc(gh2_ready, 1)
                if after(k, h):
                    squares(*after(k, h))
                for b in range(BATCHES):
                    dve.wait_ge(gh2_ready, k * (4 * BATCHES) + 2 * (h + 1) * BATCHES)
                    dve.wait_ge(ww_ps, batches_done(k, h, b))
                    nc.vector.tensor_tensor(p_n[:, bs(b)], bank[b][:], g2[:, bs(b)], ALU.add).then_inc(p2_ready, 1)
                for b in range(BATCHES):
                    dve.wait_ge(pp2_ps, batches_done(k, h, b))
                    nc.vector.tensor_tensor(q_n[:, bs(b)], bank[b][:], h2[:, bs(b)], ALU.add).then_inc(q_ready, 1)
                if after(k, h):
                    scales(*after(k, h))
                    make_a(*after(k, h))
                for b in range(BATCHES):
                    dve.wait_ge(w4_ps, batches_done(k, h, b))
                    nc.vector.scalar_tensor_tensor(t5_n[:, bs(b)], bank[b][:], -0.5 / Q_SCALE ** 2, eye_15[:],
                                                   ALU.mult, ALU.add).then_inc(t5_ready, 1)
                if not (isinstance(k, int) and k == 0):
                    dve.wait_ge(out_stored[h], k * (16 * BATCHES))
                for b in range(BATCHES):
                    dve.wait_ge(y5_ps, batches_done(k, h, b))
                    for i, m in enumerate(mm(b)):
                        ins = nc.vector.scalar_tensor_tensor(out_sb[:, h, m], bank[b][:, i], out_scale[:, h, m:m + 1],
                                                             x_sb[:, h, m], ALU.mult, ALU.add)
                    ins.then_inc(out_ready, 1)

            statistics(0, 0)
            squares(0, 0)
            scales(0, 0)
            make_a(0, 0)
            all_steps(dve, step)

        @block.tensor
        def _(pe):
            def mean_product(k, h):
                pe.wait_ge(mean_summed, steps_done(k, h))
                nc.tensor.matmul(mean_ps, mean_w[:], mean_sum[:], start=True, stop=True).then_inc(mean_ps_ready, 1)

            def sq_product(k, h):
                pe.wait_ge(sq_summed, steps_done(k, h))
                nc.tensor.matmul(sq_ps, sum_w[:], sq_row[:], start=True, stop=True).then_inc(sq_ps_ready, 1)

            def transposes(k, h, src, needs, signals):
                for b in range(BATCHES):
                    pe.wait_ge(needs, batches_done(k, h, b))
                    for i, m in enumerate(mm(b)):
                        ins = nc.tensor.transpose(bank[b][:, i], src[:, m], eye[:, 0])
                    ins.then_inc(signals, 1)

            def products(k, h, lhs_t, rhs, needs, signals):
                for b in range(BATCHES):
                    pe.wait_ge(needs, batches_done(k, h, b))
                    for i, m in enumerate(mm(b)):
                        ins = nc.tensor.matmul(bank[b][:, i], lhs_t(m), rhs(m), start=True, stop=True)
                    ins.then_inc(signals, 1)

            def step(k, h):
                prev, nxt = before(k, h), after(k, h)
                for b in range(BATCHES):
                    pe.wait_ge(a_ready, batches_done(k, h, b))
                    if prev:
                        pe.wait_ge(out_ready, batches_done(*prev, b))
                    for i, m in enumerate(mm(b)):
                        ins = nc.tensor.transpose(bank[b][:, i], a_n[:, m], eye[:, 0])
                    ins.then_inc(at_ps, 1)
                products(k, h, lambda m: a_t[:, m], lambda m: a_n[:, m], at_ready, aa_ps)
                transposes(k, h, p_n, p1_ready, pt1_ps)
                products(k, h, lambda m: p_t[:, m], lambda m: p_n[:, m], pt1_ready, pp1_ps)
                products(k, h, lambda m: z_n[:, m], lambda m: a_t[:, m], z_ready, y2t_ps)
                products(k, h, lambda m: wy_t[:, m, 1], lambda m: z_n[:, m], y2t_ready, w2_ps)
                transposes(k, h, w_n, w_ready, wt_ps)
                if nxt:
                    mean_product(*nxt)
                products(k, h, lambda m: wy_t[:, m, 0], lambda m: w_n[:, m], wt_ready, ww_ps)
                transposes(k, h, p_n, p2_ready, pt2_ps)
                if nxt:
                    sq_product(*nxt)
                products(k, h, lambda m: p_t[:, m], lambda m: p_n[:, m], pt2_ready, pp2_ps)
                for b in range(BATCHES):
                    pe.wait_ge(q_ready, batches_done(k, h, b))
                    if b >= 2:
                        pe.wait_ge(vy_ready, k * (4 * BATCHES) + (2 * (h * BATCHES + b - 2) + 2))
                    for i, m in enumerate(mm(b)):
                        ps = (bank[b], extra[b])[i // 2]
                        half = (i % 2) * 2
                        ins = nc.tensor.matmul(ps[:, half:half + 2], q_n[:, m], wy_t[:, m], start=True, stop=True)
                    ins.then_inc(vy_ps, 1)
                for b in range(BATCHES):
                    pe.wait_ge(vy_ready, k * (4 * BATCHES) + (2 * (h * BATCHES + b) + 2))
                    for i, m in enumerate(mm(b)):
                        ins = nc.tensor.matmul(bank[b][:, i], vy_t[:, m, 0], q_n[:, m], start=True, stop=True)
                    ins.then_inc(w4_ps, 1)
                products(k, h, lambda m: vy_t[:, m, 1], lambda m: t5_n[:, m], t5_ready, y5_ps)

            pe.wait_ge(consts_ready, 2)
            mean_product(0, 0)
            sq_product(0, 0)
            pe.wait_ge(eye_ready, 1)
            all_steps(pe, step)


_INS = ['x']
_OUTS = [((32, 32, 128, 128), 'float32')]


def kernel(**inputs):
    import numpy as _np
    import concourse.bacc as _bacc
    from concourse import mybir as _mybir
    from concourse.bass_utils import run_bass_kernel_spmd as _run

    nc = _bacc.Bacc("TRN2", target_bir_lowering=False, num_devices=1)
    arrays, args = {}, []
    for name in _INS:
        a = _np.ascontiguousarray(inputs[name])
        arrays[f"in_{name}_dram"] = a
        args.append(nc.dram_tensor(f"in_{name}_dram", a.shape, _mybir.dt.from_np(a.dtype), kind="ExternalInput").ap())
    for i, (shape, dtype) in enumerate(_OUTS):
        dt = _mybir.dt.from_np(_np.dtype(dtype))
        args.append(nc.dram_tensor(f"out_{i}_dram", shape, dt, kind="ExternalOutput").ap())
    newton_schulz_kernel(nc, *args)
    r = _run(nc, [arrays], core_ids=[0])
    got = tuple(r.results[0][f"out_{i}_dram"] for i in range(len(_OUTS)))
    return got[0]
```

```python
from contextlib import ExitStack

import concourse.bass as bass
from concourse import mybir

F32 = mybir.dt.float32
ALU = mybir.AluOpType
ACT = mybir.ActivationFunctionType
AX_X = mybir.AxisListType.X

N = 128
BATCH_MATS = 4
BATCHES = 4
STEP_MATS = BATCH_MATS * BATCHES
GROUP_MATS = 2
GROUPS = STEP_MATS // GROUP_MATS
GN_EPS = 1e-5
SQUARE = 32
SQUARES = N // SQUARE
PAIR = 2
BN = 6

P1, P0 = -4.5, 3.375
H1, H0 = -8.625, 24.609375
Q_SCALE = 16.0


def newton_schulz_kernel(nc, x, out):
    mats = x.shape[0] * x.shape[1]
    steps = mats // STEP_MATS
    pairs = steps // 2
    assert steps % 2 == 0 and pairs >= 3 and x.shape[2] == x.shape[3] == N

    x_dram = x.rearrange("b c i j -> (b c) i j").rearrange("(k h m) i j -> k h i m j", h=2, m=STEP_MATS)
    out_dram = out.rearrange("b c i j -> (b c) i j").rearrange("(k h m) i j -> k h i m j", h=2, m=STEP_MATS)

    with ExitStack() as ctx:
        def sb(name, shape, dt=F32):
            return ctx.enter_context(nc.sbuf_tensor(name, shape, dt))

        def sem(name):
            return ctx.enter_context(nc.semaphore(name))

        x_sb = sb("x_sb", [N, 2, STEP_MATS, N])
        out_sb = sb("out_sb", [N, 2, STEP_MATS, N])
        a_n = sb("a_n", [N, STEP_MATS, N])
        a_blocks = sb("a_blocks", [N, STEP_MATS // PAIR, SQUARES, SQUARE, PAIR])
        a_t_pairs = sb("a_t_pairs", [N, STEP_MATS // PAIR, N, PAIR])
        g1 = sb("g1", [N, STEP_MATS, N])
        h1 = sb("h1", [N, STEP_MATS, N])
        p_n = sb("p_n", [N, STEP_MATS, N])
        p_t = sb("p_t", [N, STEP_MATS, N])
        z_n = sb("z_n", [N, STEP_MATS, N])
        wy_t = sb("wy_t", [N, STEP_MATS, 2, N])
        w_n = sb("w_n", [N, STEP_MATS, N])
        g2 = sb("g2", [N, STEP_MATS, N])
        h2 = sb("h2", [N, STEP_MATS, N])
        q_n = sb("q_n", [N, STEP_MATS, N])
        vy_t = sb("vy_t", [N, STEP_MATS, 2, N])
        t5_n = g2
        eye = sb("eye", [N, BATCH_MATS, N])
        eye_p0 = sb("eye_p0", [N, BATCH_MATS, N])
        eye_h0 = sb("eye_h0", [N, BATCH_MATS, N])
        eye_15 = sb("eye_15", [N, BATCH_MATS, N])
        mean_w = sb("mean_w", [N, N])
        sum_w = sb("sum_w", [N, N])

        stats = sb("stats", [N, STEP_MATS, BN])
        mean_sum = sb("mean_sum", [N, GROUPS])
        mean = sb("mean", [N, GROUPS])
        dev = sb("dev", [N, GROUPS, 4])
        dev_sq = sb("dev_sq", [N, GROUPS, 4])
        sq_part = sb("sq_part", [N, GROUPS, 4])
        sq_row = sb("sq_row", [N, STEP_MATS])
        var_eps = sb("var_eps", [N, GROUPS])
        group_sq = sb("group_sq", [N, GROUPS])
        roots_sq = sb("roots_sq", [N, STEP_MATS + GROUPS])
        roots_0 = sb("roots_0", [N, STEP_MATS + GROUPS])
        roots_inv = sb("roots_inv", [N, STEP_MATS + GROUPS])
        roots_quot = sb("roots_quot", [N, STEP_MATS + GROUPS])
        roots_2x = sb("roots_2x", [N, STEP_MATS + GROUPS])
        half_inv = sb("half_inv", [N, STEP_MATS])
        a_scale = sb("a_scale", [N, STEP_MATS])
        fourth_0 = sb("fourth_0", [N, STEP_MATS])
        fourth_inv = sb("fourth_inv", [N, STEP_MATS])
        fourth_quot = sb("fourth_quot", [N, STEP_MATS])
        fourth_sum = sb("fourth_sum", [N, STEP_MATS])
        out_scale = sb("out_scale", [N, 2, STEP_MATS])

        bank = [ctx.enter_context(nc.psum_tensor(f"bank{i}", [N, BATCH_MATS, N], F32)) for i in range(8)]
        extra = [bank[BATCHES + b % 3] for b in range(BATCHES)]
        mean_ps = bank[7][:, 1, 0:GROUPS]
        sq_ps = bank[7][:, 0, 0:STEP_MATS]

        MOVES = 16 * SQUARES * (SQUARES - 1)

        x_loaded = [[sem(f"x_loaded_{parity}_half{half}") for half in range(2)] for parity in ("even", "odd")]
        out_stored = [sem("out_stored_even"), sem("out_stored_odd")]
        consts_ready, eye_zeroed, eye_ready = sem("consts_ready"), sem("eye_zeroed"), sem("eye_ready")
        blocks_ready, diagonal_ready = sem("blocks_ready"), sem("diagonal_ready")
        at_moved = sem("at_moved")
        at_ps, at_ready = sem("at_ps"), sem("at_ready")
        aa_ps, p1_ready = sem("aa_ps"), sem("p1_ready")
        pt1_ps, pt1_ready = sem("pt1_ps"), sem("pt1_ready")
        pp1_ps, z_ready = sem("pp1_ps"), sem("z_ready")
        y2t_ps, y2t_ready = sem("y2t_ps"), sem("y2t_ready")
        w2_ps, w_ready = sem("w2_ps"), sem("w_ready")
        wt_ps, wt_ready = sem("wt_ps"), sem("wt_ready")
        ww_ps, p2_ready = sem("ww_ps"), sem("p2_ready")
        pt2_ps, pt2_ready = sem("pt2_ps"), sem("pt2_ready")
        pp2_ps, q_ready = sem("pp2_ps"), sem("q_ready")
        vy_ps, vy_ready = sem("vy_ps"), sem("vy_ready")
        w4_ps, t5_ready = sem("w4_ps"), sem("t5_ready")
        y5_ps, out_ready = sem("y5_ps"), sem("out_ready")
        g1_scaled, h1_scaled, g1_ready, h1_ready = sem("g1_scaled"), sem("h1_scaled"), sem("g1_ready"), sem("h1_ready")
        g2_ready, h2_scaled, h2_ready = sem("g2_ready"), sem("h2_scaled"), sem("h2_ready")
        a_ready = sem("a_ready")
        stats_done, mean_summed, mean_ps_ready = sem("stats_done"), sem("mean_summed"), sem("mean_ps_ready")
        small = sem("small")
        sq_summed, sq_ps_ready = sem("sq_summed"), sem("sq_ps_ready")
        roots_in, roots_out = sem("roots_in"), sem("roots_out")
        norm_ready, fourth_out = sem("norm_ready"), sem("fourth_out")

        def mm(b):
            return range(b * BATCH_MATS, (b + 1) * BATCH_MATS)

        def bs(b):
            return slice(b * BATCH_MATS, (b + 1) * BATCH_MATS)

        def block_of(tile, i, j):
            return tile[i * SQUARE:(i + 1) * SQUARE, :, j].rearrange("r g c e -> r g (c e)")

        def square_of(tile, i, j):
            return tile[i * SQUARE:(i + 1) * SQUARE, :, j * SQUARE:(j + 1) * SQUARE, :].rearrange("r g c e -> r g (c e)")

        def batches_done(k, h, b):
            return k * (2 * BATCHES) + (h * BATCHES + b + 1)

        def steps_done(k, h):
            return k * 2 + (h + 1)

        def before(k, h):
            if h == 1:
                return k, 0
            return None if isinstance(k, int) and k == 0 else (k - 1, 1)

        def after(k, h):
            if h == 0:
                return k, 1
            return None if isinstance(k, int) and k == pairs - 1 else (k + 1, 0)

        def all_steps(eng, step):
            for h in range(2):
                step(0, h)
            with eng.Fori(1, pairs - 1) as k:
                for h in range(2):
                    step(k, h)
            for h in range(2):
                step(pairs - 1, h)

        block = ctx.enter_context(nc.Block())

        @block.sync
        def _(sp):
            def load(k, h, b):
                sp.dma_start(x_sb[:, h, bs(b)], x_dram[k, h, :, bs(b)]).then_inc(x_loaded[h][b // 2], 16)

            for h in range(2):
                for b in range(BATCHES):
                    load(0, h, b)

            def transpose_a(k, h):
                sp.wait_ge(blocks_ready, steps_done(*before(k, h)))
                for i in range(SQUARES):
                    for j in range(SQUARES):
                        if i != j:
                            sp.dma_start(square_of(a_t_pairs, j, i), block_of(a_blocks, i, j)).then_inc(at_moved, 16)

            def step(k, h):
                if after(k, h):
                    transpose_a(*after(k, h))
                for b in range(BATCHES):
                    sp.wait_ge(out_ready, batches_done(k, h, b))
                    sp.dma_start(out_dram[k, h, :, bs(b)], out_sb[:, h, bs(b)]).then_inc(out_stored[h], 16)
                    if not (isinstance(k, int) and k == pairs - 1):
                        load(k + 1, h, b)

            all_steps(sp, step)
            for h in range(2):
                sp.wait_ge(out_stored[h], 16 * BATCHES * pairs)

        @block.gpsimd
        def _(pool):
            nc.gpsimd.memset(eye[:], 0.0).then_inc(eye_zeroed, 1)
            pool.wait_ge(eye_zeroed, 1)
            nc.gpsimd.affine_select(out=eye[:], in_=eye[:], compare_op=ALU.not_equal, fill=1.0, base=0,
                                    pattern=[[0, BATCH_MATS], [-1, N]], channel_multiplier=1).then_inc(eye_ready, 1)
            pool.wait_ge(consts_ready, 5)

            def plus_eye(k, h, b, tile, eye_multiple, scaled, ready):
                pool.wait_ge(scaled, batches_done(k, h, b))
                nc.gpsimd.tensor_tensor(tile[:, bs(b)], tile[:, bs(b)], eye_multiple[:], ALU.add).then_inc(ready, 1)

            def poly_terms(k, h):
                for half in range(2):
                    for b in (2 * half, 2 * half + 1):
                        plus_eye(k, h, b, g1, eye_p0, g1_scaled, g1_ready)
                    for b in (2 * half, 2 * half + 1):
                        plus_eye(k, h, b, h1, eye_h0, h1_scaled, h1_ready)

            poly_terms(0, 0)

            def step(k, h):
                for b in range(BATCHES):
                    plus_eye(k, h, b, h2, eye_h0, h2_scaled, h2_ready)
                if after(k, h):
                    poly_terms(*after(k, h))

            all_steps(pool, step)

        @block.scalar
        def _(act):
            def roots(k, h):
                done = steps_done(k, h)
                act.wait_ge(roots_in, done)
                nc.scalar.activation(roots_0[:], roots_sq[:], ACT.Sqrt).then_inc(roots_out, 1)

            def fourth_roots(k, h):
                act.wait_ge(norm_ready, steps_done(k, h))
                nc.scalar.activation(fourth_0[:], roots_2x[:, 0:STEP_MATS], ACT.Sqrt, scale=0.5).then_inc(fourth_out, 1)

            def copies(k, h, src_ps, dst, ready, scale=1.0, batches=range(BATCHES)):
                for b in batches:
                    act.wait_ge(src_ps, batches_done(k, h, b))
                    nc.scalar.activation(dst(b), bank[b][:], ACT.Copy, scale=scale).then_inc(ready, 1)

            def diagonal_blocks(k, h):
                act.wait_ge(blocks_ready, steps_done(*before(k, h)))
                for i in range(SQUARES):
                    nc.scalar.activation(square_of(a_t_pairs, i, i), block_of(a_blocks, i, i), ACT.Copy).then_inc(diagonal_ready, 1)

            def poly_multiples(k, h, half):
                prev = before(k, h)
                for b in (2 * half, 2 * half + 1):
                    act.wait_ge(a_ready, batches_done(k, h, b))
                    if prev:
                        act.wait_ge(p1_ready, batches_done(*prev, b))
                    nc.scalar.activation(g1[:, bs(b)], a_n[:, bs(b)], ACT.Copy, scale=P1).then_inc(g1_scaled, 1)
                for b in (2 * half, 2 * half + 1):
                    if prev:
                        act.wait_ge(z_ready, batches_done(*prev, b))
                    nc.scalar.activation(h1[:, bs(b)], a_n[:, bs(b)], ACT.Copy, scale=H1).then_inc(h1_scaled, 1)

            def a_t_of_batch(b):
                pairs_of_b = slice(b * BATCH_MATS // PAIR, (b + 1) * BATCH_MATS // PAIR)
                return a_t_pairs[:, pairs_of_b].rearrange("p g c e -> p g e c")

            def vy_copies(k, h, batches):
                for b in batches:
                    act.wait_ge(vy_ps, batches_done(k, h, b))
                    for i, ps in enumerate((bank[b], extra[b])):
                        m0 = b * BATCH_MATS + 2 * i
                        nc.scalar.activation(vy_t[:, m0:m0 + 2].rearrange("p m c j -> p (m c) j"), ps[:],
                                             ACT.Copy).then_inc(vy_ready, 1)

            def step(k, h):
                nxt = after(k, h)
                copies(k, h, pt1_ps, lambda b: p_t[:, bs(b)], pt1_ready)
                copies(k, h, y2t_ps, lambda b: wy_t[:, bs(b), 1], y2t_ready)
                copies(k, h, w2_ps, lambda b: w_n[:, bs(b)], w_ready, 1.0 / Q_SCALE ** 2, [0, 1, 2])
                if nxt:
                    roots(*nxt)
                copies(k, h, w2_ps, lambda b: w_n[:, bs(b)], w_ready, 1.0 / Q_SCALE ** 2, [3])
                copies(k, h, wt_ps, lambda b: wy_t[:, bs(b), 0], wt_ready)
                if nxt:
                    fourth_roots(*nxt)
                act.wait_ge(w_ready, batches_done(k, h, BATCHES - 1))
                for b in range(BATCHES):
                    nc.scalar.activation(h2[:, bs(b)], w_n[:, bs(b)], ACT.Copy, scale=H1).then_inc(h2_scaled, 1)
                copies(k, h, pt2_ps, lambda b: p_t[:, bs(b)], pt2_ready)
                if nxt:
                    poly_multiples(*nxt, 0)
                vy_copies(k, h, [0, 1])
                if nxt:
                    diagonal_blocks(*nxt)
                vy_copies(k, h, [2, 3])
                if nxt:
                    poly_multiples(*nxt, 1)

            roots(0, 0)
            fourth_roots(0, 0)
            copies(0, 0, at_ps, a_t_of_batch, at_ready)
            for half in range(2):
                poly_multiples(0, 0, half)
            all_steps(act, step)

        @block.vector
        def _(dve):
            nc.vector.memset(mean_w[:], 1.0 / (4 * N)).then_inc(consts_ready, 1)
            nc.vector.memset(sum_w[:], 1.0).then_inc(consts_ready, 1)
            dve.wait_ge(eye_ready, 1)
            for tile, value in ((eye_p0, P0), (eye_h0, H0), (eye_15, 1.5)):
                nc.vector.tensor_scalar(tile[:], eye[:], value, None, ALU.mult).then_inc(consts_ready, 1)
            dve.wait_ge(consts_ready, 5)

            SMALLS = 15

            def statistics(k, h, half):
                mats = range(half * STEP_MATS // 2, (half + 1) * STEP_MATS // 2)
                dve.wait_ge(x_loaded[h][half], k * (16 * BATCHES // 2) + 16 * BATCHES // 2)
                for m in mats:
                    nc.vector.bn_stats(stats[:, m], x_sb[:, h, m]).then_inc(stats_done, 1)
                if half == 1:
                    dve.wait_ge(stats_done, k * (2 * STEP_MATS) + (h + 1) * STEP_MATS)
                    parts = stats[:].rearrange("p (g c) (r s) -> p g (c r) s", c=GROUP_MATS, s=3)
                    nc.vector.tensor_reduce(mean_sum[:], parts[:, :, :, 1], AX_X, ALU.add).then_inc(mean_summed, 1)


            def squares(i, k, h):
                base = k * (2 * SMALLS) + h * SMALLS
                parts = stats[:].rearrange("p (g c) (r s) -> p g (c r) s", c=GROUP_MATS, s=3)
                if i == 0:
                    dve.wait_ge(mean_ps_ready, steps_done(k, h))
                    nc.vector.tensor_copy(mean[:], mean_ps).then_inc(small, 1)
                elif i == 1:
                    dve.wait_ge(small, base + 1)
                    nc.vector.tensor_tensor(dev[:], parts[:, :, :, 1], mean[:].unsqueeze(2).broadcast_to([N, GROUPS, 4]),
                                            ALU.subtract).then_inc(small, 1)
                elif i == 2:
                    dve.wait_ge(small, base + 2)
                    nc.vector.scalar_tensor_tensor(dev_sq[:], dev[:], float(N // 2), dev[:], ALU.mult, ALU.mult).then_inc(small, 1)
                elif i == 3:
                    dve.wait_ge(small, base + 3)
                    nc.vector.tensor_tensor(sq_part[:], parts[:, :, :, 2], dev_sq[:], ALU.add).then_inc(small, 1)
                else:
                    dve.wait_ge(small, base + 4)
                    nc.vector.tensor_reduce(sq_row[:], sq_part[:].rearrange("p g (c r) -> p (g c) r", r=2),
                                            AX_X, ALU.add).then_inc(sq_summed, 1)

            def scales(i, k, h):
                base = k * (2 * SMALLS) + h * SMALLS
                norms, rstd = slice(0, STEP_MATS), slice(STEP_MATS, STEP_MATS + GROUPS)
                by_group = sq_ps.rearrange("p (g c) -> p g c", c=GROUP_MATS)

                def of_mats(tile_ap):
                    return tile_ap.rearrange("p (g c) -> p g c", c=GROUP_MATS)

                def spread(tile_ap):
                    return tile_ap.unsqueeze(2).broadcast_to([N, GROUPS, GROUP_MATS])

                if i == 0:
                    dve.wait_ge(sq_ps_ready, steps_done(k, h))
                    nc.vector.tensor_reduce(group_sq[:], by_group, AX_X, ALU.add).then_inc(small, 1)
                elif i == 1:
                    dve.wait_ge(small, base + 5)
                    nc.vector.tensor_scalar(var_eps[:], group_sq[:], 1.0 / (GROUP_MATS * N * N), GN_EPS,
                                            ALU.mult, ALU.add).then_inc(small, 1)
                elif i == 2:
                    dve.wait_ge(small, base + 6)
                    nc.vector.reciprocal(roots_sq[:, rstd], var_eps[:]).then_inc(small, 1)
                elif i == 3:
                    dve.wait_ge(small, base + 7)
                    nc.vector.tensor_tensor(of_mats(roots_sq[:, norms]), by_group, spread(roots_sq[:, rstd]),
                                            ALU.mult).then_inc(roots_in, 1)
                elif i == 4:
                    dve.wait_ge(roots_out, steps_done(k, h))
                    nc.vector.reciprocal(roots_inv[:], roots_0[:]).then_inc(small, 1)
                elif i == 5:
                    dve.wait_ge(small, base + 8)
                    nc.vector.tensor_tensor(roots_quot[:], roots_sq[:], roots_inv[:], ALU.mult).then_inc(small, 1)
                elif i == 6:
                    dve.wait_ge(small, base + 9)
                    nc.vector.tensor_tensor(roots_2x[:], roots_quot[:], roots_0[:], ALU.add).then_inc(norm_ready, 1)
                elif i == 7:
                    dve.wait_ge(norm_ready, steps_done(k, h))
                    nc.vector.reciprocal(half_inv[:], roots_2x[:, norms]).then_inc(small, 1)
                elif i == 8:
                    dve.wait_ge(small, base + 10)
                    nc.vector.tensor_tensor(of_mats(a_scale[:]), of_mats(half_inv[:]), spread(roots_2x[:, rstd]),
                                            ALU.mult).then_inc(small, 1)
                elif i == 9:
                    dve.wait_ge(fourth_out, steps_done(k, h))
                    nc.vector.reciprocal(fourth_inv[:], fourth_0[:]).then_inc(small, 1)
                elif i == 10:
                    dve.wait_ge(small, base + 12)
                    nc.vector.scalar_tensor_tensor(fourth_quot[:], roots_2x[:, norms], 0.5, fourth_inv[:],
                                                   ALU.mult, ALU.mult).then_inc(small, 1)
                elif i == 11:
                    dve.wait_ge(small, base + 13)
                    nc.vector.tensor_tensor(fourth_sum[:], fourth_quot[:], fourth_0[:], ALU.add).then_inc(small, 1)
                else:
                    dve.wait_ge(small, base + 14)
                    nc.vector.tensor_scalar(out_scale[:, h], fourth_sum[:], 0.5 / Q_SCALE ** 2, None, ALU.mult).then_inc(small, 1)

            def make_a(k, h, mats):
                dve.wait_ge(small, k * (2 * SMALLS) + (h * SMALLS + 11))
                for m in mats:
                    g = m // GROUP_MATS
                    ins = nc.vector.tensor_scalar(a_n[:, m], x_sb[:, h, m], mean[:, g:g + 1], a_scale[:, m:m + 1],
                                                  ALU.subtract, ALU.mult)
                    if m % BATCH_MATS == BATCH_MATS - 1:
                        ins.then_inc(a_ready, 1)

            def transpose_blocks(k, h, b):
                dve.wait_ge(a_ready, batches_done(k, h, b))
                for g in range(b * BATCH_MATS // PAIR, (b + 1) * BATCH_MATS // PAIR):
                    ins = nc.vector.transpose(a_blocks[:, g].rearrange("p j c e -> p e j c"),
                                              a_n[:, g * PAIR:(g + 1) * PAIR].rearrange("p e (j c) -> p e j c", c=SQUARE))
                if b == BATCHES - 1:
                    ins.then_inc(blocks_ready, 1)

            def q_from_banks(k, h, b):
                dve.wait_ge(h2_ready, batches_done(k, h, b))
                dve.wait_ge(pp2_ps, batches_done(k, h, b))
                nc.vector.tensor_tensor(q_n[:, bs(b)], bank[b][:], h2[:, bs(b)], ALU.add).then_inc(q_ready, 1)

            def step(k, h):
                nxt = after(k, h)
                for b in range(BATCHES):
                    dve.wait_ge(g1_ready, batches_done(k, h, b))
                    dve.wait_ge(aa_ps, batches_done(k, h, b))
                    nc.vector.tensor_tensor(p_n[:, bs(b)], bank[b][:], g1[:, bs(b)], ALU.add).then_inc(p1_ready, 1)
                if nxt:
                    statistics(*nxt, 0)
                for b in range(BATCHES):
                    dve.wait_ge(h1_ready, batches_done(k, h, b))
                    dve.wait_ge(pp1_ps, batches_done(k, h, b))
                    nc.vector.tensor_tensor(z_n[:, bs(b)], bank[b][:], h1[:, bs(b)], ALU.add).then_inc(z_ready, 1)
                if nxt:
                    statistics(*nxt, 1)
                    for i in range(5):
                        squares(i, *nxt)
                for b in range(BATCHES):
                    dve.wait_ge(w_ready, batches_done(k, h, b))
                    nc.vector.scalar_tensor_tensor(g2[:, bs(b)], w_n[:, bs(b)], P1, eye_p0[:], ALU.mult, ALU.add).then_inc(g2_ready, 1)
                    if nxt:
                        for i in ((0, 1, 2, 3), (4, 5), (6, 7), (8,))[b]:
                            scales(i, *nxt)
                if nxt:
                    make_a(*nxt, [0, 1])
                dve.wait_ge(g2_ready, batches_done(k, h, BATCHES - 1))
                for b in range(BATCHES):
                    dve.wait_ge(ww_ps, batches_done(k, h, b))
                    nc.vector.tensor_tensor(p_n[:, bs(b)], bank[b][:], g2[:, bs(b)], ALU.add).then_inc(p2_ready, 1)
                    if nxt and b < 3:
                        make_a(*nxt, [b + 2])
                if nxt:
                    make_a(*nxt, [5, 6, 7])
                    transpose_blocks(*nxt, 0)
                q_from_banks(k, h, 0)
                if nxt:
                    transpose_blocks(*nxt, 1)
                q_from_banks(k, h, 1)
                q_from_banks(k, h, 2)
                if nxt:
                    for b in (2, 3):
                        make_a(*nxt, mm(b))
                        transpose_blocks(*nxt, b)
                q_from_banks(k, h, 3)
                if nxt:
                    for i in range(9, 13):
                        scales(i, *nxt)
                for b in range(BATCHES):
                    dve.wait_ge(w4_ps, batches_done(k, h, b))
                    nc.vector.scalar_tensor_tensor(t5_n[:, bs(b)], bank[b][:], -0.5 / Q_SCALE ** 2, eye_15[:],
                                                   ALU.mult, ALU.add).then_inc(t5_ready, 1)
                if not (isinstance(k, int) and k == 0):
                    dve.wait_ge(out_stored[h], k * (16 * BATCHES))
                for b in range(BATCHES):
                    dve.wait_ge(y5_ps, batches_done(k, h, b))
                    for i, m in enumerate(mm(b)):
                        ins = nc.vector.scalar_tensor_tensor(out_sb[:, h, m], bank[b][:, i], out_scale[:, h, m:m + 1],
                                                             x_sb[:, h, m], ALU.mult, ALU.add)
                    ins.then_inc(out_ready, 1)

            statistics(0, 0, 0)
            statistics(0, 0, 1)
            for i in range(5):
                squares(i, 0, 0)
            for i in range(9):
                scales(i, 0, 0)
            make_a(0, 0, range(STEP_MATS))
            for i in range(9, 13):
                scales(i, 0, 0)
            all_steps(dve, step)

        @block.tensor
        def _(pe):
            def mean_product(k, h):
                pe.wait_ge(mean_summed, steps_done(k, h))
                nc.tensor.matmul(mean_ps, mean_w[:], mean_sum[:], start=True, stop=True).then_inc(mean_ps_ready, 1)

            def sq_product(k, h):
                pe.wait_ge(sq_summed, steps_done(k, h))
                nc.tensor.matmul(sq_ps, sum_w[:], sq_row[:], start=True, stop=True).then_inc(sq_ps_ready, 1)

            def transposes(k, h, src, needs, signals):
                for b in range(BATCHES):
                    pe.wait_ge(needs, batches_done(k, h, b))
                    for i, m in enumerate(mm(b)):
                        ins = nc.tensor.transpose(bank[b][:, i], src[:, m], eye[:, 0])
                    ins.then_inc(signals, 1)

            def products(k, h, lhs_t, rhs, needs, signals, batches=range(BATCHES)):
                for b in batches:
                    pe.wait_ge(needs, batches_done(k, h, b))
                    for i, m in enumerate(mm(b)):
                        ins = nc.tensor.matmul(bank[b][:, i], lhs_t(m), rhs(m), start=True, stop=True)
                    ins.then_inc(signals, 1)

            def a_t(m):
                return a_t_pairs[:, m // PAIR, :, m % PAIR]

            def step(k, h):
                prev, nxt = before(k, h), after(k, h)
                for b in range(BATCHES):
                    if not prev:
                        pe.wait_ge(at_ready, b + 1)
                    elif b == 0:
                        pe.wait_ge(diagonal_ready, k * (2 * SQUARES) + h * SQUARES)
                        pe.wait_ge(at_moved, k * (2 * MOVES) + h * MOVES)
                    if prev:
                        pe.wait_ge(out_ready, batches_done(*prev, b))
                    for i, m in enumerate(mm(b)):
                        ins = nc.tensor.matmul(bank[b][:, i], a_t(m), a_n[:, m], start=True, stop=True)
                    ins.then_inc(aa_ps, 1)
                transposes(k, h, p_n, p1_ready, pt1_ps)
                products(k, h, lambda m: p_t[:, m], lambda m: p_n[:, m], pt1_ready, pp1_ps)
                products(k, h, lambda m: z_n[:, m], a_t, z_ready, y2t_ps)
                if nxt:
                    mean_product(*nxt)
                products(k, h, lambda m: wy_t[:, m, 1], lambda m: z_n[:, m], y2t_ready, w2_ps, [0, 1])
                if nxt:
                    sq_product(*nxt)
                products(k, h, lambda m: wy_t[:, m, 1], lambda m: z_n[:, m], y2t_ready, w2_ps, [2, 3])
                transposes(k, h, w_n, w_ready, wt_ps)
                products(k, h, lambda m: wy_t[:, m, 0], lambda m: w_n[:, m], wt_ready, ww_ps)
                transposes(k, h, p_n, p2_ready, pt2_ps)
                products(k, h, lambda m: p_t[:, m], lambda m: p_n[:, m], pt2_ready, pp2_ps)
                for b in range(BATCHES):
                    pe.wait_ge(q_ready, batches_done(k, h, b))
                    if b >= 3:
                        pe.wait_ge(vy_ready, k * (4 * BATCHES) + 2 * (h * BATCHES + b - 2))
                    for i, m in enumerate(mm(b)):
                        ps = (bank[b], extra[b])[i // 2]
                        half = (i % 2) * 2
                        ins = nc.tensor.matmul(ps[:, half:half + 2], q_n[:, m], wy_t[:, m], start=True, stop=True)
                    ins.then_inc(vy_ps, 1)
                for b in range(BATCHES):
                    pe.wait_ge(vy_ready, k * (4 * BATCHES) + (2 * (h * BATCHES + b) + 2))
                    for i, m in enumerate(mm(b)):
                        ins = nc.tensor.matmul(bank[b][:, i], vy_t[:, m, 0], q_n[:, m], start=True, stop=True)
                    ins.then_inc(w4_ps, 1)
                products(k, h, lambda m: vy_t[:, m, 1], lambda m: t5_n[:, m], t5_ready, y5_ps)

            assert BATCHES == 4
            pe.wait_ge(consts_ready, 2)
            mean_product(0, 0)
            sq_product(0, 0)
            pe.wait_ge(eye_ready, 1)
            transposes(0, 0, a_n, a_ready, at_ps)
            all_steps(pe, step)


_INS = ['x']
_OUTS = [((32, 32, 128, 128), 'float32')]


def kernel(**inputs):
    import numpy as _np
    import concourse.bacc as _bacc
    from concourse import mybir as _mybir
    from concourse.bass_utils import run_bass_kernel_spmd as _run

    nc = _bacc.Bacc("TRN2", target_bir_lowering=False, num_devices=1)
    arrays, args = {}, []
    for name in _INS:
        a = _np.ascontiguousarray(inputs[name])
        arrays[f"in_{name}_dram"] = a
        args.append(nc.dram_tensor(f"in_{name}_dram", a.shape, _mybir.dt.from_np(a.dtype), kind="ExternalInput").ap())
    for i, (shape, dtype) in enumerate(_OUTS):
        dt = _mybir.dt.from_np(_np.dtype(dtype))
        args.append(nc.dram_tensor(f"out_{i}_dram", shape, dt, kind="ExternalOutput").ap())
    newton_schulz_kernel(nc, *args)
    r = _run(nc, [arrays], core_ids=[0])
    got = tuple(r.results[0][f"out_{i}_dram"] for i in range(len(_OUTS)))
    return got[0]
```

```python
from contextlib import ExitStack

import concourse.bass as bass
from concourse import mybir

F32 = mybir.dt.float32
ALU = mybir.AluOpType
ACT = mybir.ActivationFunctionType
AX_X = mybir.AxisListType.X

N = 128
BATCH_MATS = 4
BATCHES = 4
STEP_MATS = BATCH_MATS * BATCHES
SLOTS = 4
GROUP_MATS = 2
GROUPS = STEP_MATS // GROUP_MATS
GN_EPS = 1e-5
SQUARE = 32
SQUARES = N // SQUARE
PAIR = 2
BN = 6

P1, P0 = -4.5, 3.375
H1, H0 = -8.625, 24.609375
Q_SCALE = 16.0


def newton_schulz_kernel(nc, x, out):
    mats = x.shape[0] * x.shape[1]
    rounds = mats // STEP_MATS // SLOTS
    assert mats % (STEP_MATS * SLOTS) == 0 and rounds >= 3 and x.shape[2] == x.shape[3] == N

    x_dram = x.rearrange("b c i j -> (b c) i j").rearrange("(k h m) i j -> k h i m j", h=SLOTS, m=STEP_MATS)
    out_dram = out.rearrange("b c i j -> (b c) i j").rearrange("(k h m) i j -> k h i m j", h=SLOTS, m=STEP_MATS)

    with ExitStack() as ctx:
        def sb(name, shape, dt=F32):
            return ctx.enter_context(nc.sbuf_tensor(name, shape, dt))

        def sem(name):
            return ctx.enter_context(nc.semaphore(name))

        x_sb = sb("x_sb", [N, SLOTS, STEP_MATS, N])
        a_n = sb("a_n", [N, STEP_MATS, N])
        blocks = sb("blocks", [N, STEP_MATS // PAIR, SQUARES, SQUARE, PAIR])
        a_t_pairs = sb("a_t_pairs", [N, STEP_MATS // PAIR, N, PAIR])
        g1 = sb("g1", [N, STEP_MATS, N])
        h1 = sb("h1", [N, STEP_MATS, N])
        p_n = sb("p_n", [N, STEP_MATS, N])
        p_t_pairs = sb("p_t_pairs", [N, STEP_MATS // PAIR, N, PAIR])
        z_n = sb("z_n", [N, STEP_MATS, N])
        wy_t = sb("wy_t", [N, STEP_MATS, 2, N])
        w_n = sb("w_n", [N, STEP_MATS, N])
        g2 = sb("g2", [N, STEP_MATS, N])
        h2 = sb("h2", [N, STEP_MATS, N])
        q_n = sb("q_n", [N, STEP_MATS, N])
        vy_t = sb("vy_t", [N, STEP_MATS, 2, N])
        t5_n = g2
        eye = sb("eye", [N, BATCH_MATS, N])
        eye_p0 = sb("eye_p0", [N, BATCH_MATS, N])
        eye_h0 = sb("eye_h0", [N, BATCH_MATS, N])
        eye_15 = sb("eye_15", [N, BATCH_MATS, N])
        mean_w = sb("mean_w", [N, N])
        sum_w = sb("sum_w", [N, N])

        stats = sb("stats", [N, STEP_MATS, BN])
        mean_sum = sb("mean_sum", [N, GROUPS])
        mean = sb("mean", [N, GROUPS])
        dev = sb("dev", [N, GROUPS, 4])
        dev_sq = sb("dev_sq", [N, GROUPS, 4])
        sq_part = sb("sq_part", [N, GROUPS, 4])
        sq_row = sb("sq_row", [N, STEP_MATS])
        var_eps = sb("var_eps", [N, GROUPS])
        group_sq = sb("group_sq", [N, GROUPS])
        roots_sq = sb("roots_sq", [N, STEP_MATS + GROUPS])
        roots_0 = sb("roots_0", [N, STEP_MATS + GROUPS])
        roots_inv = sb("roots_inv", [N, STEP_MATS + GROUPS])
        roots_quot = sb("roots_quot", [N, STEP_MATS + GROUPS])
        roots_2x = sb("roots_2x", [N, STEP_MATS + GROUPS])
        half_inv = sb("half_inv", [N, STEP_MATS])
        a_scale = sb("a_scale", [N, STEP_MATS])
        fourth_0 = sb("fourth_0", [N, STEP_MATS])
        fourth_inv = sb("fourth_inv", [N, STEP_MATS])
        fourth_quot = sb("fourth_quot", [N, STEP_MATS])
        fourth_sum = sb("fourth_sum", [N, STEP_MATS])
        out_scale = sb("out_scale", [N, SLOTS, STEP_MATS])

        bank = [ctx.enter_context(nc.psum_tensor(f"bank{i}", [N, BATCH_MATS, N], F32)) for i in range(8)]
        extra = [bank[BATCHES + b % 3] for b in range(BATCHES)]
        mean_ps = bank[7][:, 1, 0:GROUPS]
        sq_ps = bank[7][:, 0, 0:STEP_MATS]

        MOVES = 16 * SQUARES * (SQUARES - 1)

        x_loaded = [sem(f"x_loaded_{slot}") for slot in range(SLOTS)]
        out_stored = [sem(f"out_stored_{slot}") for slot in range(SLOTS)]
        consts_ready, eye_zeroed, eye_ready = sem("consts_ready"), sem("eye_zeroed"), sem("eye_ready")
        a_blocks_ready, a_diagonal_ready, at_moved = sem("a_blocks_ready"), sem("a_diagonal_ready"), sem("at_moved")
        p_blocks_ready, p_diagonal_ready, pt_moved = sem("p_blocks_ready"), sem("p_diagonal_ready"), sem("pt_moved")
        at_ps, at_ready, pt1_ps, pt1_ready = sem("at_ps"), sem("at_ready"), sem("pt1_ps"), sem("pt1_ready")
        aa_ps, p1_ready = sem("aa_ps"), sem("p1_ready")
        pp1_ps, z_ready = sem("pp1_ps"), sem("z_ready")
        y2t_ps, y2t_ready = sem("y2t_ps"), sem("y2t_ready")
        w2_ps, w_ready = sem("w2_ps"), sem("w_ready")
        wt_ps, wt_ready = sem("wt_ps"), sem("wt_ready")
        ww_ps, p2_ready = sem("ww_ps"), sem("p2_ready")
        pt2_ps, pt2_ready = sem("pt2_ps"), sem("pt2_ready")
        pp2_ps, q_ready = sem("pp2_ps"), sem("q_ready")
        vy_ps, vy_ready = sem("vy_ps"), sem("vy_ready")
        w4_ps, t5_ready = sem("w4_ps"), sem("t5_ready")
        y5_ps, out_ready = sem("y5_ps"), sem("out_ready")
        g1_scaled, h1_scaled, g1_ready, h1_ready = sem("g1_scaled"), sem("h1_scaled"), sem("g1_ready"), sem("h1_ready")
        g2_ready, h2_scaled, h2_ready = sem("g2_ready"), sem("h2_scaled"), sem("h2_ready")
        a_ready = sem("a_ready")
        stats_done, mean_summed, mean_ps_ready = sem("stats_done"), sem("mean_summed"), sem("mean_ps_ready")
        small = sem("small")
        sq_summed, sq_ps_ready = sem("sq_summed"), sem("sq_ps_ready")
        roots_in, roots_out = sem("roots_in"), sem("roots_out")
        norm_ready, fourth_out = sem("norm_ready"), sem("fourth_out")

        def mm(b):
            return range(b * BATCH_MATS, (b + 1) * BATCH_MATS)

        def bs(b):
            return slice(b * BATCH_MATS, (b + 1) * BATCH_MATS)

        def block_of(i, j):
            return blocks[i * SQUARE:(i + 1) * SQUARE, :, j].rearrange("r g c e -> r g (c e)")

        def square_of(tile, i, j):
            return tile[i * SQUARE:(i + 1) * SQUARE, :, j * SQUARE:(j + 1) * SQUARE, :].rearrange("r g c e -> r g (c e)")

        def paired_batch(tile, b):
            g0 = b * BATCH_MATS // PAIR
            return tile[:, g0:g0 + BATCH_MATS // PAIR].rearrange("p g c e -> p g e c")

        def a_t(m):
            return a_t_pairs[:, m // PAIR, :, m % PAIR]

        def p_t(m):
            return p_t_pairs[:, m // PAIR, :, m % PAIR]

        def batches_done(k, h, b):
            return k * (SLOTS * BATCHES) + (h * BATCHES + b + 1)

        def steps_done(k, h):
            return k * SLOTS + (h + 1)

        def before(k, h):
            if h > 0:
                return k, h - 1
            return None if isinstance(k, int) and k == 0 else (k - 1, SLOTS - 1)

        def after(k, h, ahead=1):
            if h + ahead < SLOTS:
                return k, h + ahead
            return None if isinstance(k, int) and k == rounds - 1 else (k + 1, h + ahead - SLOTS)

        def all_steps(eng, step):
            for h in range(SLOTS):
                step(0, h)
            with eng.Fori(1, rounds - 1) as k:
                for h in range(SLOTS):
                    step(k, h)
            for h in range(SLOTS):
                step(rounds - 1, h)

        block = ctx.enter_context(nc.Block())

        @block.sync
        def _(sp):
            def load(k, h):
                for b in range(BATCHES):
                    sp.dma_start(x_sb[:, h, bs(b)], x_dram[k, h, :, bs(b)]).then_inc(x_loaded[h], 16)

            def move_blocks(dst, moved):
                for i in range(SQUARES):
                    for j in range(SQUARES):
                        if i != j:
                            sp.dma_start(square_of(dst, j, i), block_of(i, j)).then_inc(moved, 16)

            for h in range(SLOTS - 1):
                load(0, h)

            def step(k, h):
                if after(k, h):
                    sp.wait_ge(a_blocks_ready, steps_done(k, h))
                    move_blocks(a_t_pairs, at_moved)
                if after(k, h, 3):
                    prev = before(k, h)
                    if prev:
                        sp.wait_ge(out_stored[prev[1]], prev[0] * (16 * BATCHES) + 16 * BATCHES)
                    load(*after(k, h, 3))
                if after(k, h):
                    sp.wait_ge(p_blocks_ready, steps_done(k, h))
                    move_blocks(p_t_pairs, pt_moved)
                for b in (1, 0, 2, 3):
                    if b > 0:
                        sp.wait_ge(out_ready, batches_done(k, h, b))
                    sp.dma_start(out_dram[k, h, :, bs(b)], x_sb[:, h, bs(b)]).then_inc(out_stored[h], 16)

            all_steps(sp, step)
            for h in range(SLOTS):
                sp.wait_ge(out_stored[h], 16 * BATCHES * rounds)

        @block.gpsimd
        def _(pool):
            nc.gpsimd.memset(eye[:], 0.0).then_inc(eye_zeroed, 1)
            pool.wait_ge(eye_zeroed, 1)
            nc.gpsimd.affine_select(out=eye[:], in_=eye[:], compare_op=ALU.not_equal, fill=1.0, base=0,
                                    pattern=[[0, BATCH_MATS], [-1, N]], channel_multiplier=1).then_inc(eye_ready, 1)
            pool.wait_ge(consts_ready, 5)

            def plus_eye(k, h, b, tile, eye_multiple, scaled, ready):
                pool.wait_ge(scaled, batches_done(k, h, b))
                nc.gpsimd.tensor_tensor(tile[:, bs(b)], tile[:, bs(b)], eye_multiple[:], ALU.add).then_inc(ready, 1)

            def g_of_a(k, h):
                for b in range(BATCHES):
                    plus_eye(k, h, b, g1, eye_p0, g1_scaled, g1_ready)

            def h_of_a(k, h):
                for b in range(BATCHES):
                    plus_eye(k, h, b, h1, eye_h0, h1_scaled, h1_ready)

            g_of_a(0, 0)
            h_of_a(0, 0)
            g_of_a(0, 1)

            def step(k, h):
                for b in range(BATCHES):
                    plus_eye(k, h, b, h2, eye_h0, h2_scaled, h2_ready)
                if after(k, h):
                    h_of_a(*after(k, h))
                if after(k, h, 2):
                    g_of_a(*after(k, h, 2))

            all_steps(pool, step)

        @block.scalar
        def _(act):
            def roots(k, h):
                done = steps_done(k, h)
                act.wait_ge(roots_in, done)
                nc.scalar.activation(roots_0[:], roots_sq[:], ACT.Sqrt).then_inc(roots_out, 1)

            def fourth_roots(k, h):
                act.wait_ge(norm_ready, steps_done(k, h))
                nc.scalar.activation(fourth_0[:], roots_2x[:, 0:STEP_MATS], ACT.Sqrt, scale=0.5).then_inc(fourth_out, 1)

            def copies(k, h, src_ps, dst, ready, scale=1.0, batches=range(BATCHES)):
                for b in batches:
                    act.wait_ge(src_ps, batches_done(k, h, b))
                    nc.scalar.activation(dst(b), bank[b][:], ACT.Copy, scale=scale).then_inc(ready, 1)

            def diagonal_blocks(k, h, dst, blocks_ready, ready):
                act.wait_ge(blocks_ready, steps_done(*before(k, h)))
                for i in range(SQUARES):
                    nc.scalar.activation(square_of(dst, i, i), block_of(i, i), ACT.Copy).then_inc(ready, 1)

            def multiples_for_g(k, h):
                prev = before(k, h)
                for b in range(BATCHES):
                    act.wait_ge(a_ready, batches_done(k, h, b))
                    if prev:
                        act.wait_ge(p1_ready, batches_done(*prev, b))
                    nc.scalar.activation(g1[:, bs(b)], a_n[:, bs(b)], ACT.Copy, scale=P1).then_inc(g1_scaled, 1)

            def multiples_for_h(k, h):
                prev = before(k, h)
                for b in range(BATCHES):
                    if prev:
                        act.wait_ge(z_ready, batches_done(*prev, b))
                    nc.scalar.activation(h1[:, bs(b)], a_n[:, bs(b)], ACT.Copy, scale=H1).then_inc(h1_scaled, 1)

            def vy_copies(k, h, batches):
                for b in batches:
                    act.wait_ge(vy_ps, batches_done(k, h, b))
                    for i, ps in enumerate((bank[b], extra[b])):
                        m0 = b * BATCH_MATS + 2 * i
                        nc.scalar.activation(vy_t[:, m0:m0 + 2].rearrange("p m c j -> p (m c) j"), ps[:],
                                             ACT.Copy).then_inc(vy_ready, 1)

            def step(k, h):
                nxt, nxt2 = after(k, h), after(k, h, 2)
                copies(k, h, y2t_ps, lambda b: wy_t[:, bs(b), 1], y2t_ready)
                if not before(k, h):
                    multiples_for_g(*nxt)
                copies(k, h, w2_ps, lambda b: w_n[:, bs(b)], w_ready, 1.0 / Q_SCALE ** 2)
                copies(k, h, wt_ps, lambda b: wy_t[:, bs(b), 0], wt_ready)
                act.wait_ge(w_ready, batches_done(k, h, BATCHES - 1))
                for b in range(BATCHES):
                    nc.scalar.activation(h2[:, bs(b)], w_n[:, bs(b)], ACT.Copy, scale=H1).then_inc(h2_scaled, 1)
                copies(k, h, pt2_ps, lambda b: paired_batch(p_t_pairs, b), pt2_ready)
                if nxt:
                    diagonal_blocks(*nxt, a_t_pairs, a_blocks_ready, a_diagonal_ready)
                    multiples_for_h(*nxt)
                if nxt2:
                    roots(*nxt2)
                vy_copies(k, h, [0])
                if nxt2:
                    fourth_roots(*nxt2)
                vy_copies(k, h, [1])
                if nxt:
                    diagonal_blocks(*nxt, p_t_pairs, p_blocks_ready, p_diagonal_ready)
                vy_copies(k, h, [2, 3])
                if nxt2:
                    multiples_for_g(*nxt2)

            roots(0, 0)
            fourth_roots(0, 0)
            copies(0, 0, at_ps, lambda b: paired_batch(a_t_pairs, b), at_ready)
            multiples_for_g(0, 0)
            multiples_for_h(0, 0)
            copies(0, 0, pt1_ps, lambda b: paired_batch(p_t_pairs, b), pt1_ready)
            roots(0, 1)
            fourth_roots(0, 1)
            all_steps(act, step)

        @block.vector
        def _(dve):
            nc.vector.memset(mean_w[:], 1.0 / (4 * N)).then_inc(consts_ready, 1)
            nc.vector.memset(sum_w[:], 1.0).then_inc(consts_ready, 1)
            dve.wait_ge(eye_ready, 1)
            for tile, value in ((eye_p0, P0), (eye_h0, H0), (eye_15, 1.5)):
                nc.vector.tensor_scalar(tile[:], eye[:], value, None, ALU.mult).then_inc(consts_ready, 1)
            dve.wait_ge(consts_ready, 5)

            SMALLS = 15

            def statistics(k, h, mats):
                dve.wait_ge(x_loaded[h], k * (16 * BATCHES) + 16 * BATCHES)
                for m in mats:
                    nc.vector.bn_stats(stats[:, m], x_sb[:, h, m]).then_inc(stats_done, 1)
                if m == STEP_MATS - 1:
                    dve.wait_ge(stats_done, steps_done(k, h) * STEP_MATS)
                    parts = stats[:].rearrange("p (g c) (r s) -> p g (c r) s", c=GROUP_MATS, s=3)
                    nc.vector.tensor_reduce(mean_sum[:], parts[:, :, :, 1], AX_X, ALU.add).then_inc(mean_summed, 1)


            def squares(i, k, h):
                base = k * (SLOTS * SMALLS) + h * SMALLS
                parts = stats[:].rearrange("p (g c) (r s) -> p g (c r) s", c=GROUP_MATS, s=3)
                if i == 0:
                    dve.wait_ge(mean_ps_ready, steps_done(k, h))
                    nc.vector.tensor_copy(mean[:], mean_ps).then_inc(small, 1)
                elif i == 1:
                    dve.wait_ge(small, base + 1)
                    nc.vector.tensor_tensor(dev[:], parts[:, :, :, 1], mean[:].unsqueeze(2).broadcast_to([N, GROUPS, 4]),
                                            ALU.subtract).then_inc(small, 1)
                elif i == 2:
                    dve.wait_ge(small, base + 2)
                    nc.vector.scalar_tensor_tensor(dev_sq[:], dev[:], float(N // 2), dev[:], ALU.mult, ALU.mult).then_inc(small, 1)
                elif i == 3:
                    dve.wait_ge(small, base + 3)
                    nc.vector.tensor_tensor(sq_part[:], parts[:, :, :, 2], dev_sq[:], ALU.add).then_inc(small, 1)
                else:
                    dve.wait_ge(small, base + 4)
                    nc.vector.tensor_reduce(sq_row[:], sq_part[:].rearrange("p g (c r) -> p (g c) r", r=2),
                                            AX_X, ALU.add).then_inc(sq_summed, 1)

            def scales(i, k, h):
                base = k * (SLOTS * SMALLS) + h * SMALLS
                norms, rstd = slice(0, STEP_MATS), slice(STEP_MATS, STEP_MATS + GROUPS)
                by_group = sq_ps.rearrange("p (g c) -> p g c", c=GROUP_MATS)

                def of_mats(tile_ap):
                    return tile_ap.rearrange("p (g c) -> p g c", c=GROUP_MATS)

                def spread(tile_ap):
                    return tile_ap.unsqueeze(2).broadcast_to([N, GROUPS, GROUP_MATS])

                if i == 0:
                    dve.wait_ge(sq_ps_ready, steps_done(k, h))
                    nc.vector.tensor_reduce(group_sq[:], by_group, AX_X, ALU.add).then_inc(small, 1)
                elif i == 1:
                    dve.wait_ge(small, base + 5)
                    nc.vector.tensor_scalar(var_eps[:], group_sq[:], 1.0 / (GROUP_MATS * N * N), GN_EPS,
                                            ALU.mult, ALU.add).then_inc(small, 1)
                elif i == 2:
                    dve.wait_ge(small, base + 6)
                    nc.vector.reciprocal(roots_sq[:, rstd], var_eps[:]).then_inc(small, 1)
                elif i == 3:
                    dve.wait_ge(small, base + 7)
                    nc.vector.tensor_tensor(of_mats(roots_sq[:, norms]), by_group, spread(roots_sq[:, rstd]),
                                            ALU.mult).then_inc(roots_in, 1)
                elif i == 4:
                    dve.wait_ge(roots_out, steps_done(k, h))
                    nc.vector.reciprocal(roots_inv[:], roots_0[:]).then_inc(small, 1)
                elif i == 5:
                    dve.wait_ge(small, base + 8)
                    nc.vector.tensor_tensor(roots_quot[:], roots_sq[:], roots_inv[:], ALU.mult).then_inc(small, 1)
                elif i == 6:
                    dve.wait_ge(small, base + 9)
                    nc.vector.tensor_tensor(roots_2x[:], roots_quot[:], roots_0[:], ALU.add).then_inc(norm_ready, 1)
                elif i == 7:
                    dve.wait_ge(norm_ready, steps_done(k, h))
                    nc.vector.reciprocal(half_inv[:], roots_2x[:, norms]).then_inc(small, 1)
                elif i == 8:
                    dve.wait_ge(small, base + 10)
                    nc.vector.tensor_tensor(of_mats(a_scale[:]), of_mats(half_inv[:]), spread(roots_2x[:, rstd]),
                                            ALU.mult).then_inc(small, 1)
                elif i == 9:
                    dve.wait_ge(fourth_out, steps_done(k, h))
                    nc.vector.reciprocal(fourth_inv[:], fourth_0[:]).then_inc(small, 1)
                elif i == 10:
                    dve.wait_ge(small, base + 12)
                    nc.vector.scalar_tensor_tensor(fourth_quot[:], roots_2x[:, norms], 0.5, fourth_inv[:],
                                                   ALU.mult, ALU.mult).then_inc(small, 1)
                elif i == 11:
                    dve.wait_ge(small, base + 13)
                    nc.vector.tensor_tensor(fourth_sum[:], fourth_quot[:], fourth_0[:], ALU.add).then_inc(small, 1)
                else:
                    dve.wait_ge(small, base + 14)
                    nc.vector.tensor_scalar(out_scale[:, h], fourth_sum[:], 0.5 / Q_SCALE ** 2, None, ALU.mult).then_inc(small, 1)

            def make_a(k, h, mats=range(STEP_MATS)):
                dve.wait_ge(small, k * (SLOTS * SMALLS) + (h * SMALLS + 11))
                for m in mats:
                    if before(k, h) and m % BATCH_MATS == 0:
                        dve.wait_ge(h1_scaled, batches_done(*before(k, h), m // BATCH_MATS))
                    g = m // GROUP_MATS
                    ins = nc.vector.tensor_scalar(a_n[:, m], x_sb[:, h, m], mean[:, g:g + 1], a_scale[:, m:m + 1],
                                                  ALU.subtract, ALU.mult)
                    if m % BATCH_MATS == BATCH_MATS - 1:
                        ins.then_inc(a_ready, 1)

            def transpose_blocks(k, h, b, src, needs, signals):
                dve.wait_ge(needs, batches_done(k, h, b))
                for g in range(b * BATCH_MATS // PAIR, (b + 1) * BATCH_MATS // PAIR):
                    ins = nc.vector.transpose(blocks[:, g].rearrange("p j c e -> p e j c"),
                                              src[:, g * PAIR:(g + 1) * PAIR].rearrange("p e (j c) -> p e j c", c=SQUARE))
                if b == BATCHES - 1:
                    ins.then_inc(signals, 1)

            def p_from_banks(k, h, b):
                dve.wait_ge(g1_ready, batches_done(k, h, b))
                dve.wait_ge(aa_ps, batches_done(k, h, b))
                nc.vector.tensor_tensor(p_n[:, bs(b)], bank[b][:], g1[:, bs(b)], ALU.add).then_inc(p1_ready, 1)

            def q_from_banks(k, h, b):
                dve.wait_ge(h2_ready, batches_done(k, h, b))
                dve.wait_ge(pp2_ps, batches_done(k, h, b))
                nc.vector.tensor_tensor(q_n[:, bs(b)], bank[b][:], h2[:, bs(b)], ALU.add).then_inc(q_ready, 1)

            def step(k, h):
                nxt, nxt2 = after(k, h), after(k, h, 2)
                for b in range(BATCHES):
                    dve.wait_ge(h1_ready, batches_done(k, h, b))
                    dve.wait_ge(pp1_ps, batches_done(k, h, b))
                    nc.vector.tensor_tensor(z_n[:, bs(b)], bank[b][:], h1[:, bs(b)], ALU.add).then_inc(z_ready, 1)
                if not before(k, h):
                    make_a(*nxt)
                if nxt:
                    for b in range(BATCHES):
                        if b == BATCHES - 1:
                            if nxt2:
                                statistics(*nxt2, range(0, 4))
                            dve.wait_ge(y2t_ps, batches_done(k, h, BATCHES - 1))
                        transpose_blocks(*nxt, b, a_n, a_ready, a_blocks_ready)
                if nxt2:
                    statistics(*nxt2, range(4, 8))
                for b in range(BATCHES):
                    dve.wait_ge(w_ready, batches_done(k, h, b))
                    nc.vector.scalar_tensor_tensor(g2[:, bs(b)], w_n[:, bs(b)], P1, eye_p0[:], ALU.mult, ALU.add).then_inc(g2_ready, 1)
                if nxt2:
                    statistics(*nxt2, range(8, 14))
                dve.wait_ge(g2_ready, batches_done(k, h, BATCHES - 1))
                for b in range(BATCHES):
                    dve.wait_ge(ww_ps, batches_done(k, h, b))
                    nc.vector.tensor_tensor(p_n[:, bs(b)], bank[b][:], g2[:, bs(b)], ALU.add).then_inc(p2_ready, 1)
                    if nxt2 and b < 2:
                        statistics(*nxt2, [14 + b])
                if nxt2:
                    for i in range(5):
                        squares(i, *nxt2)
                for b in range(BATCHES):
                    q_from_banks(k, h, b)
                    if nxt2:
                        for i in ((), (0, 1), (2,), (3,))[b]:
                            scales(i, *nxt2)
                if nxt:
                    for b in range(BATCHES):
                        p_from_banks(*nxt, b)
                        if nxt2:
                            scales(b + 4, *nxt2)
                        transpose_blocks(*nxt, b, p_n, p1_ready, p_blocks_ready)
                if nxt2:
                    scales(8, *nxt2)
                    make_a(*nxt2)
                for b in range(BATCHES):
                    dve.wait_ge(w4_ps, batches_done(k, h, b))
                    nc.vector.scalar_tensor_tensor(t5_n[:, bs(b)], bank[b][:], -0.5 / Q_SCALE ** 2, eye_15[:],
                                                   ALU.mult, ALU.add).then_inc(t5_ready, 1)
                    if nxt2:
                        scales(b + 9, *nxt2)
                for b in range(BATCHES):
                    dve.wait_ge(y5_ps, batches_done(k, h, b))
                    for i, m in enumerate(mm(b)):
                        ins = nc.vector.scalar_tensor_tensor(x_sb[:, h, m], bank[b][:, i], out_scale[:, h, m:m + 1],
                                                             x_sb[:, h, m], ALU.mult, ALU.add)
                    ins.then_inc(out_ready, 1)

            statistics(0, 0, range(STEP_MATS))
            for i in range(5):
                squares(i, 0, 0)
            for i in range(9):
                scales(i, 0, 0)
            make_a(0, 0)
            for i in range(9, 13):
                scales(i, 0, 0)
            statistics(0, 1, range(STEP_MATS))
            for b in range(BATCHES):
                p_from_banks(0, 0, b)
            for i in range(5):
                squares(i, 0, 1)
            for i in range(13):
                scales(i, 0, 1)
            all_steps(dve, step)

        @block.tensor
        def _(pe):
            def mean_product(k, h):
                pe.wait_ge(mean_summed, steps_done(k, h))
                nc.tensor.matmul(mean_ps, mean_w[:], mean_sum[:], start=True, stop=True).then_inc(mean_ps_ready, 1)

            def sq_product(k, h):
                pe.wait_ge(sq_summed, steps_done(k, h))
                nc.tensor.matmul(sq_ps, sum_w[:], sq_row[:], start=True, stop=True).then_inc(sq_ps_ready, 1)

            def transposes(k, h, src, needs, signals):
                for b in range(BATCHES):
                    pe.wait_ge(needs, batches_done(k, h, b))
                    for i, m in enumerate(mm(b)):
                        ins = nc.tensor.transpose(bank[b][:, i], src[:, m], eye[:, 0])
                    ins.then_inc(signals, 1)

            def products(k, h, lhs_t, rhs, needs, signals, batches=range(BATCHES)):
                for b in batches:
                    pe.wait_ge(needs, batches_done(k, h, b))
                    for i, m in enumerate(mm(b)):
                        ins = nc.tensor.matmul(bank[b][:, i], lhs_t(m), rhs(m), start=True, stop=True)
                    ins.then_inc(signals, 1)

            def a_a(k, h):
                prev = before(k, h)
                if prev:
                    pe.wait_ge(a_diagonal_ready, steps_done(*prev) * SQUARES)
                    pe.wait_ge(at_moved, steps_done(*prev) * MOVES)
                for b in range(BATCHES):
                    if prev:
                        pe.wait_ge(q_ready, batches_done(*prev, b))
                    else:
                        pe.wait_ge(at_ready, b + 1)
                    for i, m in enumerate(mm(b)):
                        ins = nc.tensor.matmul(bank[b][:, i], a_t(m), a_n[:, m], start=True, stop=True)
                    ins.then_inc(aa_ps, 1)

            def step(k, h):
                prev, nxt, nxt2 = before(k, h), after(k, h), after(k, h, 2)
                if prev:
                    pe.wait_ge(p_diagonal_ready, steps_done(*prev) * SQUARES)
                    pe.wait_ge(pt_moved, steps_done(*prev) * MOVES)
                for b in range(BATCHES):
                    if prev:
                        pe.wait_ge(out_ready, batches_done(*prev, b))
                    else:
                        pe.wait_ge(pt1_ready, b + 1)
                    for i, m in enumerate(mm(b)):
                        ins = nc.tensor.matmul(bank[b][:, i], p_t(m), p_n[:, m], start=True, stop=True)
                    ins.then_inc(pp1_ps, 1)
                products(k, h, lambda m: z_n[:, m], a_t, z_ready, y2t_ps)
                products(k, h, lambda m: wy_t[:, m, 1], lambda m: z_n[:, m], y2t_ready, w2_ps)
                transposes(k, h, w_n, w_ready, wt_ps)
                products(k, h, lambda m: wy_t[:, m, 0], lambda m: w_n[:, m], wt_ready, ww_ps)
                transposes(k, h, p_n, p2_ready, pt2_ps)
                if nxt2:
                    mean_product(*nxt2)
                products(k, h, p_t, lambda m: p_n[:, m], pt2_ready, pp2_ps, [0, 1])
                if nxt2:
                    sq_product(*nxt2)
                products(k, h, p_t, lambda m: p_n[:, m], pt2_ready, pp2_ps, [2, 3])
                if nxt:
                    a_a(*nxt)
                for b in range(BATCHES):
                    if nxt:
                        pe.wait_ge(p1_ready, batches_done(*nxt, b))
                    pe.wait_ge(q_ready, batches_done(k, h, b))
                    if b >= 3:
                        pe.wait_ge(vy_ready, 2 * batches_done(k, h, b - 3))
                    for i, m in enumerate(mm(b)):
                        ps = (bank[b], extra[b])[i // 2]
                        half = (i % 2) * 2
                        ins = nc.tensor.matmul(ps[:, half:half + 2], q_n[:, m], wy_t[:, m], start=True, stop=True)
                    ins.then_inc(vy_ps, 1)
                for b in range(BATCHES):
                    pe.wait_ge(vy_ready, 2 * batches_done(k, h, b))
                    for i, m in enumerate(mm(b)):
                        ins = nc.tensor.matmul(bank[b][:, i], vy_t[:, m, 0], q_n[:, m], start=True, stop=True)
                    ins.then_inc(w4_ps, 1)
                products(k, h, lambda m: vy_t[:, m, 1], lambda m: t5_n[:, m], t5_ready, y5_ps)

            assert BATCHES == 4
            pe.wait_ge(consts_ready, 2)
            mean_product(0, 0)
            sq_product(0, 0)
            pe.wait_ge(eye_ready, 1)
            transposes(0, 0, a_n, a_ready, at_ps)
            a_a(0, 0)
            mean_product(0, 1)
            transposes(0, 0, p_n, p1_ready, pt1_ps)
            sq_product(0, 1)
            all_steps(pe, step)


_INS = ['x']
_OUTS = [((32, 32, 128, 128), 'float32')]


def kernel(**inputs):
    import numpy as _np
    import concourse.bacc as _bacc
    from concourse import mybir as _mybir
    from concourse.bass_utils import run_bass_kernel_spmd as _run

    nc = _bacc.Bacc("TRN2", target_bir_lowering=False, num_devices=1)
    arrays, args = {}, []
    for name in _INS:
        a = _np.ascontiguousarray(inputs[name])
        arrays[f"in_{name}_dram"] = a
        args.append(nc.dram_tensor(f"in_{name}_dram", a.shape, _mybir.dt.from_np(a.dtype), kind="ExternalInput").ap())
    for i, (shape, dtype) in enumerate(_OUTS):
        dt = _mybir.dt.from_np(_np.dtype(dtype))
        args.append(nc.dram_tensor(f"out_{i}_dram", shape, dt, kind="ExternalOutput").ap())
    newton_schulz_kernel(nc, *args)
    r = _run(nc, [arrays], core_ids=[0])
    got = tuple(r.results[0][f"out_{i}_dram"] for i in range(len(_OUTS)))
    return got[0]
```
